# Optimizing a Trainium2 kernel written in Bass

```python
import numpy as np
import jax
import jax.numpy as jnp

def _softmax(x, axis=-1):
    return jax.nn.softmax(x, axis=axis)
def _gelu(x):
    return jax.nn.gelu(x, approximate=True)
def _silu(x):
    return jax.nn.silu(x)
def _sigmoid(x):
    return jax.nn.sigmoid(x)
def _layernorm(x, axis=-1, eps=1e-5):
    m = jnp.mean(x, axis=axis, keepdims=True)
    v = jnp.var(x, axis=axis, keepdims=True)
    return (x - m) / jnp.sqrt(v + eps)
def _scatter_add(tgt, idx, src, axis=0):
    return tgt.at[idx].add(src)
def _segment_sum(src, seg, n):
    return jax.ops.segment_sum(src, seg, n)

kernel_name = 'mk_adj_resnorm_d1_adj_512_8852c8'

def setup_inputs(seed: int = 0):
    np.random.seed(seed)
    _w = jnp.asarray
    def _rec_inputs():
        import jax
        import jax.numpy as jnp
        _gk = jax.random.key(seed)
        x = -0.000929 + 1 * jax.random.normal(jax.random.fold_in(_gk, 1), (8, 2048, 512), jnp.float32)
        _a = jax.random.bernoulli(jax.random.fold_in(_gk, 2), 0.0078125, (2048, 2048))
        adj = _a.astype(jnp.int32)
        return x, adj
    x, adj = _rec_inputs()
    def _L0_gnn_setup():
        import jax, jax.numpy as jnp
        import numpy as np
        B, K, DIN, DOUT = (32, 64, 512, 512)
        key = jax.random.key(seed)
        k1, k2, k3, k4 = jax.random.split(key, 4)
        x = jax.random.normal(k1, (B, K, DIN), dtype=jnp.float32)
        adj = jax.random.randint(k2, (K, K), 0, 2, dtype=jnp.int32)
        W = jax.random.normal(k3, (DOUT, 2 * DIN), dtype=jnp.float32) * 0.02
        b = jax.random.normal(k4, (DOUT,), dtype=jnp.float32) * 0.02
        return {'x': x, 'adj': adj, 'W': W, 'b': b}
    _L0_gnn_all = _L0_gnn_setup()
    _L0_gnn_in = {k: v for k, v in _L0_gnn_all.items() if k in ('W', 'b', )}
    del _L0_gnn_all

    return {
        "x": x,
        "adj": adj,
        "L0_gnn_W": _L0_gnn_in["W"],
        "L0_gnn_b": _L0_gnn_in["b"],
    }

def reference(x, adj, L0_gnn_W, L0_gnn_b):
    import jax
    import jax.numpy as jnp
    def _L0_gnn_ref(x, adj, W, b):
        import jax, jax.numpy as jnp
        import numpy as np
        B, K, DIN, DOUT = (32, 64, 512, 512)
        Din = x.shape[-1]
        Wi, Wj = (W[:, :Din], W[:, Din:])
        mi = jnp.einsum('bkd,od->bko', x, Wi)
        mj = jnp.einsum('bkd,od->bko', x, Wj)
        a = adj.astype(x.dtype)
        deg = a.sum(axis=1)
        out = deg[None, :, None] * (mi + b) + jnp.einsum('ij,bjo->bio', a, mj)
        return out

    x = _layernorm(x + _L0_gnn_ref(x, adj, L0_gnn_W, L0_gnn_b), axis=-1)
    return x


_drawn_inputs = setup_inputs


def setup_inputs(seed=0):
    import zlib

    import numpy as np

    out = dict(_drawn_inputs(seed))
    spreads = {}
    factors = {}
    for name, (base, spread) in spreads.items():
        noise = np.random.default_rng([zlib.crc32(name.encode()), seed]).standard_normal(out[name].shape)
        drawn = base * np.exp(spread * noise) if base else spread * noise
        out[name] = jnp.asarray(drawn.astype(out[name].dtype))
    for name, factor in factors.items():
        out[name] = (out[name] * factor).astype(out[name].dtype)
    return out
```

```python
import concourse.bass as bass
from concourse import mybir
from contextlib import ExitStack


def bass_adj_resnorm(nc, x, adj, W, b, out):
    fp32 = mybir.dt.float32
    fp32r = mybir.dt.float32r
    bf16 = mybir.dt.bfloat16
    i32 = mybir.dt.int32
    u32 = mybir.dt.uint32
    i8 = mybir.dt.int8
    ALU = mybir.AluOpType
    ACT = mybir.ActivationFunctionType

    NB, N, D = x.shape
    DO = W.shape[0]
    P = 128
    NT = N // P
    DK = D // P
    OT = DO // P
    GT = 4
    NG = NT // GT
    NP = NT // 2
    HALF = NT // 2
    LN = 7
    EPS = 1e-5
    HI_BITS = 0xFFFFF000

    x_pairs = x.rearrange("b (q s p) d -> (b q) p s d", s=2, p=P)
    out_pairs = out.rearrange("b (q s p) d -> (b q) p s d", s=2, p=P)
    adj_tiles = adj.rearrange("(t p) n -> t p n", p=P)
    w_rows = W.rearrange("(t p) d -> p t d", p=P)

    ctx = ExitStack()
    with ctx:
        def sb(name, shape, dt):
            return ctx.enter_context(nc.sbuf_tensor(name, shape, dt))

        def pb(name):
            return ctx.enter_context(nc.psum_tensor(name, [P, 512], fp32))

        def sem(name):
            return ctx.enter_context(nc.semaphore(name))

        adjT8 = sb("adjT8", [P, NT, NT, P], i8)
        adjT = [sb(f"adjT{s}", [P, NT, P], fp32r) for s in range(2)]
        mj_hi = sb("mj_hi", [P, NT, DO], fp32r)
        mj_lo = sb("mj_lo", [P, NT, DO], fp32r)
        r = sb("r", [P, NT, DO], fp32)
        WT = sb("WT", [P, 2 * DK, DO], fp32)
        x_in = [sb(f"x_in{s}", [P, 2, D], fp32) for s in range(2)]
        xT = [sb(f"xT{s}", [P, DK, P], fp32) for s in range(2)]
        mj_top = [sb(f"mj_top{s}", [P, DO], fp32) for s in range(2)]
        stage = sb("stage", [P, OT, 2 * D], fp32)
        adj_in = [stage[:, 2 * s:2 * s + 2, :].rearrange("p t d -> p (t d)").bitcast(i32) for s in range(2)]
        adj_bf = [sb(f"adj_bf{s}", [P, N], bf16) for s in range(2)]
        bias = sb("bias", [P, DO], fp32)
        deg = sb("deg", [P, NT], fp32)
        ident = sb("ident", [P, P], fp32)
        ident_bf = sb("ident_bf", [P, P], bf16)
        stats = sb("stats", [P, 6], fp32)
        mean_var = sb("mean_var", [P, 2], fp32)
        var_eps = sb("var_eps", [P, 1], fp32)
        std = sb("std", [P, 1], fp32)
        inv0 = sb("inv0", [P, 1], fp32)
        newton = sb("newton", [P, 2], fp32)
        inv_std = sb("inv_std", [P, 1], fp32)

        xT_ps = [pb(f"xT_ps{s}") for s in range(2)]
        mj_ps = [pb(f"mj_ps{s}") for s in range(2)]
        mi_ps = [pb(f"mi_ps{s}") for s in range(2)]
        agg_ps = [pb(f"agg_ps{s}") for s in range(2)]
        adjT_ps = [a[:, :].bitcast(bf16) for a in agg_ps]
        wT_ps = [mi_ps[0], mi_ps[1], agg_ps[0], agg_ps[1]]

        x_loaded = [sem(f"x_loaded{s}") for s in range(2)]
        w_loaded = [sem("wi_loaded"), sem("wj_loaded")]
        b_loaded = sem("b_loaded")
        adj_loaded = [sem(f"adj_loaded{s}") for s in range(2)]
        out_stored = sem("out_stored")
        zeroed = sem("zeroed")
        ident_ready = sem("ident_ready")
        wT_in_psum = sem("wT_in_psum")
        wT_even = sem("wT_even")
        wT_odd = sem("wT_odd")
        xT_in_psum = sem("xT_in_psum")
        xT_ready = sem("xT_ready")
        mj_ready = sem("mj_ready")
        mi_ready = sem("mi_ready")
        top_ready = sem("top_ready")
        hi_ready = sem("hi_ready")
        lo_ready = sem("lo_ready")
        mib_ready = sem("mib_ready")
        r_ready = sem("r_ready")
        adj_cast = sem("adj_cast")
        adjT_in_psum = sem("adjT_in_psum")
        adjT8_ready = sem("adjT8_ready")
        adjT_ready = sem("adjT_ready")
        agg_ready = sem("agg_ready")
        sum_ready = sem("sum_ready")
        ln_step = sem("ln_step")
        std_ready = sem("std_ready")
        norm_ready = sem("norm_ready")

        block = ctx.enter_context(nc.Block())

        def over_batches(eng, batch):
            batch(0)
            with eng.Fori(1, NB - 1) as bt:
                batch(bt)
            batch(NB - 1)

        def over_groups(eng, bt, group, last_apart=True):
            first = 0
            if isinstance(bt, int) and bt == 0:
                group(0)
                first = 1
            end = NG - 1 if last_apart else NG
            with eng.Fori(first, end) as g:
                group(g)
            if last_apart:
                group(NG - 1)

        def known(*v):
            return all(isinstance(a, int) for a in v)

        @block.sync
        def _(sp):
            def load_pair(q, slot):
                sp.dma_start(x_in[slot][:, :, :], x_pairs[q]).then_inc(x_loaded[slot], 16)

            def load_next(q, slot):
                sp.wait_ge(r_ready, 2 * (q - 1))
                load_pair(q, slot)

            def load_adj(t, slot):
                sp.wait_ge(adj_cast, t - 1)
                sp.dma_start(adj_in[slot], adj_tiles[t]).then_inc(adj_loaded[slot], 16)

            load_pair(0, 0)
            sp.dma_start(stage[:, :, D:], w_rows[:, :, D:]).then_inc(w_loaded[1], 16)
            sp.dma_start(stage[:, :, :D], w_rows[:, :, :D]).then_inc(w_loaded[0], 16)
            sp.dma_start(bias[:, :], b.partition_broadcast(P)).then_inc(b_loaded, 16)
            load_pair(1, 1)
            sp.wait_ge(wT_in_psum, 2 * DK)
            for slot in range(2):
                sp.dma_start(adj_in[slot], adj_tiles[slot]).then_inc(adj_loaded[slot], 16)

            def batch(bt):
                if known(bt) and bt == 0:
                    load_adj(2, 0)
                    load_adj(3, 1)
                    with sp.Fori(1, NG) as g:
                        for s in range(2):
                            load_next(2 * g + s, s)
                            for u in range(2):
                                load_adj(4 * g + 2 * s + u, u)
                else:
                    with sp.Fori(1, NG) as g:
                        for s in range(2):
                            load_next(NP * bt + 2 * g + s, s)
                if not (known(bt) and bt == NB - 1):
                    for s in range(2):
                        load_next(NP * bt + NP + s, s)
                with sp.Fori(0, NP) as k:
                    sp.wait_ge(norm_ready, NT * bt + 2 * k + 2)
                    sp.dma_start(out_pairs[NP * bt + k], r[:, bass.ds(2 * k, 2), :]).then_inc(out_stored, 16)

            over_batches(sp, batch)
            sp.wait_ge(out_stored, 16 * NP * NB)

        @block.gpsimd
        def _(pool):
            for m in (ident, ident_bf):
                pool.memset(m[:, :], 0.0).then_inc(zeroed, 1)
            pool.wait_ge(zeroed, 2)
            for m in (ident, ident_bf):
                pool.affine_select(out=m[:, :], in_=m[:, :], compare_op=ALU.not_equal, fill=1.0, base=0,
                                   pattern=[[-1, P]], channel_multiplier=1).then_inc(ident_ready, 1)

        @block.tensor
        def _(pe):
            def transpose_x(n, u, slot_value):
                if u % 2 == 0:
                    pe.wait_ge(x_loaded[u // 2], slot_value)
                for k in range(DK):
                    last = nc.tensor.transpose(xT_ps[u % 2][:, k * P:(k + 1) * P],
                                               x_in[u // 2][:, u % 2, k * P:(k + 1) * P], ident[:, :])
                last.then_inc(xT_in_psum, 1)

            def transpose_w(half):
                pe.wait_ge(w_loaded[half], 16)
                for k in range(DK):
                    if half == 0:
                        pe.wait_ge(wT_odd if k % 2 else wT_even, k // 2 + 1)
                    for t in range(OT):
                        last = nc.tensor.transpose(wT_ps[k][:, t * P:(t + 1) * P],
                                                   stage[:, t, half * D + k * P:half * D + (k + 1) * P],
                                                   ident[:, :])
                    last.then_inc(wT_in_psum, 1)

            def transpose_adj(t):
                pe.wait_ge(adj_cast, t + 1)
                for h in range(2):
                    if not (known(t) and t == 0):
                        pe.wait_ge(adjT8_ready, 2 * t - 1 + h)
                    for c in range(HALF):
                        j = h * HALF + c
                        last = nc.tensor.transpose(adjT_ps[h][:, c * P:(c + 1) * P],
                                                   adj_bf[t_slot[0]][:, j * P:(j + 1) * P], ident_bf[:, :])
                    last.then_inc(adjT_in_psum, 1)

            t_slot = [0]

            def project(n, s, dst, half, free, ready, wait_free):
                if wait_free:
                    pe.wait_ge(free, n - 1)
                for k in range(DK):
                    last = nc.tensor.matmul(dst[s][:, :], xT[s][:, k, :], WT[:, half * DK + k, :],
                                            start=(k == 0), stop=(k == DK - 1))
                last.then_inc(ready, 1)

            def aggregate(bt, i, s, first, wait_free):
                m = NT * bt + i
                if wait_free:
                    pe.wait_ge(sum_ready, m - 1)
                pe.wait_ge(adjT_ready, m + 1)
                for j in range(NT):
                    if first and j >= NT - 2:
                        n = NT * bt + j
                        pe.wait_ge(hi_ready, n + 1)
                        pe.wait_ge(lo_ready, n + 1)
                    for part in (mj_hi, mj_lo):
                        last = nc.tensor.matmul(agg_ps[s][:, :], adjT[s][:, j, :], part[:, j, :],
                                                start=(j == 0 and part is mj_hi),
                                                stop=(j == NT - 1 and part is mj_lo))
                last.then_inc(agg_ready, 1)

            def batch(bt):
                zero = known(bt) and bt == 0

                def group(g):
                    start = zero and known(g) and g == 0
                    end = known(g) and g == NG - 1
                    for u in range(GT):
                        n = NT * bt + GT * g + u
                        if not (end and u == GT - 1):
                            v = (u + 1) % GT
                            pair = NG * bt + g + (1 if v == 0 else 0)
                            transpose_x(n + 1, v, 16 * (pair + 1))
                        pe.wait_ge(xT_ready, n + 1)
                        if start and u == 0:
                            pe.wait_ge(wT_even, DK // 2)
                            pe.wait_ge(wT_odd, DK // 2)
                        project(n, u % 2, mj_ps, 1, lo_ready, mj_ready, not (start and u < 2))
                        if start and u == 0:
                            transpose_w(0)
                            pe.wait_ge(wT_even, DK)
                            pe.wait_ge(wT_odd, DK)
                        project(n, u % 2, mi_ps, 0, r_ready, mi_ready, not (start and u < 2))
                        if zero and not (start and u == 0):
                            t_slot[0] = (u - 1) % 2
                            transpose_adj(GT * g + u - 1)

                over_groups(pe, bt, group)
                if zero:
                    t_slot[0] = (NT - 1) % 2
                    transpose_adj(NT - 1)
                    pe.wait_ge(adjT8_ready, 2 * NT)

                for i in range(2):
                    aggregate(bt, i, i, i == 0, not (zero))
                with pe.Fori(1, NP - 1) as k:
                    for i in range(2):
                        aggregate(bt, 2 * k + i, i, False, True)
                if not (known(bt) and bt == NB - 1):
                    transpose_x(NT * bt + NT, 0, 16 * (NG * bt + NG + 1))
                for i in range(2):
                    aggregate(bt, NT - 2 + i, i, False, True)

            pe.wait_ge(ident_ready, 2)
            transpose_x(0, 0, 16)
            transpose_w(1)
            over_batches(pe, batch)

        @block.scalar
        def _(act):
            def copy_wT(half, k):
                act.wait_ge(wT_in_psum, (1 - half) * DK + k + 1)
                nc.scalar.activation(WT[:, half * DK + k, :], wT_ps[k][:, :], ACT.Copy).then_inc(wT_even, 1)

            def copy_xT(n, s, wait_free):
                if wait_free:
                    act.wait_ge(mi_ready, n - 1)
                act.wait_ge(xT_in_psum, n + 1)
                nc.scalar.activation(xT[s][:, :, :].rearrange("p k i -> p (k i)"), xT_ps[s][:, :],
                                     ACT.Copy).then_inc(xT_ready, 1)

            def cast_adj(t, s, wait_free):
                if wait_free:
                    act.wait_ge(adjT_in_psum, 2 * t - 2)
                act.wait_ge(adj_loaded[s], 8 * (t - s) + 16)
                nc.scalar.activation(adj_bf[s][:, :], adj_in[s], ACT.Copy,
                                     accum_out=deg[:, bass.ds(t, 1)]).then_inc(adj_cast, 1)

            def copy_hi(n, t, s):
                act.wait_ge(top_ready, n + 1)
                nc.scalar.activation(mj_hi[:, bass.ds(t, 1), :].rearrange("p t d -> p (t d)"),
                                     mj_top[s][:, :], ACT.Copy).then_inc(hi_ready, 1)

            def widen_adjT(i, s):
                nc.scalar.activation(adjT[s][:, :, :].rearrange("p t i -> p (t i)"),
                                     adjT8[:, bass.ds(i, 1), :, :].rearrange("p a t i -> p (a t i)"),
                                     ACT.Copy).then_inc(adjT_ready, 1)

            def root(m):
                act.wait_ge(ln_step, LN * m + 3)
                nc.scalar.activation(std[:, :], var_eps[:, :], ACT.Sqrt).then_inc(std_ready, 1)

            def batch(bt):
                zero = known(bt) and bt == 0

                def group(g):
                    start = zero and known(g) and g == 0
                    end = known(g) and g == NG - 1
                    if end:
                        for i in range(2):
                            if zero:
                                act.wait_ge(adjT8_ready, 2 * i + 2)
                            widen_adjT(i, i)
                    for u in range(GT):
                        n = NT * bt + GT * g + u
                        if not (end and u == GT - 1):
                            copy_xT(n + 1, (u + 1) % 2, not (start and u == 0))
                        if zero:
                            cast_adj(GT * g + u, u % 2, not (start and u < 2))
                        copy_hi(n, GT * g + u, u % 2)

                over_groups(act, bt, group)
                with act.Fori(0, NP - 1) as k:
                    for i in range(2):
                        m = NT * bt + 2 * k + i
                        act.wait_ge(agg_ready, m + 1)
                        if zero:
                            act.wait_ge(adjT8_ready, 4 * k + 2 * i + 6)
                        widen_adjT(2 * k + i + 2, i)
                        root(m)
                if not (known(bt) and bt == NB - 1):
                    copy_xT(NT * bt + NT, 0, True)
                for i in range(2):
                    root(NT * bt + NT - 2 + i)

            act.wait_ge(xT_in_psum, 1)
            nc.scalar.activation(xT[0][:, :, :].rearrange("p k i -> p (k i)"), xT_ps[0][:, :],
                                 ACT.Copy).then_inc(xT_ready, 1)
            for half in (1, 0):
                for k in range(0, DK, 2):
                    copy_wT(half, k)
            over_batches(act, batch)

        @block.vector
        def _(dve):
            def copy_wT(half, k):
                dve.wait_ge(wT_in_psum, (1 - half) * DK + k + 1)
                nc.vector.tensor_copy(WT[:, half * DK + k, :], wT_ps[k][:, :]).then_inc(wT_odd, 1)

            def slot(buf, t):
                return buf[:, bass.ds(t, 1), :].rearrange("p t d -> p (t d)")

            def split_mj(n, t, s, wait_free):
                if wait_free:
                    dve.wait_ge(hi_ready, n - 1)
                dve.wait_ge(mj_ready, n + 1)
                nc.vector.tensor_scalar(mj_top[s][:, :].bitcast(u32), mj_ps[s][:, :].bitcast(u32),
                                        HI_BITS, None, ALU.bitwise_and).then_inc(top_ready, 1)
                dve.wait_ge(top_ready, n + 1)
                nc.vector.tensor_tensor(slot(mj_lo, t), mj_ps[s][:, :], mj_top[s][:, :],
                                        ALU.subtract).then_inc(lo_ready, 1)

            def residual(n, t, u):
                dve.wait_ge(mi_ready, n + 1)
                nc.vector.tensor_tensor(slot(r, t), mi_ps[u % 2][:, :], bias[:, :], ALU.add).then_inc(mib_ready, 1)
                dve.wait_ge(mib_ready, n + 1)
                nc.vector.scalar_tensor_tensor(slot(r, t), slot(r, t), deg[:, bass.ds(t, 1)],
                                               x_in[u // 2][:, u % 2, :], ALU.mult, ALU.add).then_inc(r_ready, 1)

            def copy_adjT(t):
                for h in range(2):
                    dve.wait_ge(adjT_in_psum, 2 * t + h + 1)
                    nc.vector.tensor_copy(
                        adjT8[:, bass.ds(t, 1), h * HALF:(h + 1) * HALF, :].rearrange("p a t i -> p (a t i)"),
                        adjT_ps[h]).then_inc(adjT8_ready, 1)

            def normalise(m, i, s):
                dve.wait_ge(agg_ready, m + 1)
                nc.vector.tensor_tensor(slot(r, i), agg_ps[s][:, :], slot(r, i), ALU.add).then_inc(sum_ready, 1)
                dve.drain()
                nc.vector.bn_stats(stats[:, :], slot(r, i)).then_inc(ln_step, 1)
                dve.drain()
                nc.vector.bn_aggr(mean_var[:, :], stats[:, :]).then_inc(ln_step, 1)
                dve.wait_ge(ln_step, LN * m + 2)
                nc.vector.tensor_scalar_add(var_eps[:, :], mean_var[:, 1:2], EPS).then_inc(ln_step, 1)
                dve.wait_ge(std_ready, m + 1)
                nc.vector.reciprocal(inv0[:, :], std[:, :]).then_inc(ln_step, 1)
                dve.wait_ge(ln_step, LN * m + 4)
                nc.vector.scalar_tensor_tensor(newton[:, 0:1], inv0[:, :], var_eps[:, :], inv0[:, :],
                                               ALU.mult, ALU.mult).then_inc(ln_step, 1)
                dve.wait_ge(ln_step, LN * m + 5)
                nc.vector.tensor_scalar(newton[:, 1:2], newton[:, 0:1], -0.5, 1.5,
                                        ALU.mult, ALU.add).then_inc(ln_step, 1)
                dve.wait_ge(ln_step, LN * m + 6)
                nc.vector.tensor_tensor(inv_std[:, :], inv0[:, :], newton[:, 1:2], ALU.mult).then_inc(ln_step, 1)
                dve.wait_ge(ln_step, LN * m + 7)
                nc.vector.tensor_scalar(slot(r, i), slot(r, i), mean_var[:, 0:1], inv_std[:, :],
                                        ALU.subtract, ALU.mult).then_inc(norm_ready, 1)

            def batch(bt):
                zero = known(bt) and bt == 0

                def group(g):
                    start = zero and known(g) and g == 0
                    for u in range(GT):
                        t = GT * g + u
                        n = NT * bt + t
                        split_mj(n, t, u % 2, not (start and u < 2))
                        if start and u == 0:
                            for k in range(1, DK, 2):
                                copy_wT(0, k)
                            dve.wait_ge(b_loaded, 16)
                        if zero:
                            dve.wait_ge(adj_cast, t + 1)
                        elif u == 0:
                            dve.wait_ge(out_stored, 16 * NP * bt)
                        residual(n, t, u)
                        if zero and not (start and u == 0):
                            copy_adjT(t - 1)

                over_groups(dve, bt, group, last_apart=False)
                if zero:
                    copy_adjT(NT - 1)
                with dve.Fori(0, NP) as k:
                    for i in range(2):
                        normalise(NT * bt + 2 * k + i, 2 * k + i, i)

            for k in range(1, DK, 2):
                copy_wT(1, k)
            over_batches(dve, batch)


def kernel(**inputs):
    import numpy as _np
    import concourse.bacc as _bacc
    from concourse import mybir as _mybir
    from concourse.bass_utils import run_bass_kernel_spmd as _run

    nc = _bacc.Bacc("TRN2", target_bir_lowering=False, num_devices=1)
    arrays, args = {}, []
    for name in ("x", "adj", "L0_gnn_W", "L0_gnn_b"):
        a = _np.ascontiguousarray(inputs[name])
        arrays[f"in_{name}"] = a
        args.append(nc.dram_tensor(f"in_{name}", a.shape, _mybir.dt.from_np(a.dtype), kind="ExternalInput").ap())
    shape = arrays["in_x"].shape
    args.append(nc.dram_tensor("out_0", shape, _mybir.dt.float32, kind="ExternalOutput").ap())
    bass_adj_resnorm(nc, *args)
    r = _run(nc, [arrays], core_ids=[0])
    return r.results[0]["out_0"]
```

```python
import concourse.bass as bass
from concourse import mybir
from contextlib import ExitStack


def bass_adj_resnorm(nc, x, adj, W, b, out):
    fp32 = mybir.dt.float32
    fp32r = mybir.dt.float32r
    bf16 = mybir.dt.bfloat16
    i32 = mybir.dt.int32
    u32 = mybir.dt.uint32
    i8 = mybir.dt.int8
    ALU = mybir.AluOpType
    ACT = mybir.ActivationFunctionType

    NB, N, D = x.shape
    DO = W.shape[0]
    P = 128
    NT = N // P
    DK = D // P
    OT = DO // P
    B = 32
    Q = P // B
    GT = 4
    NG = NT // GT
    NP = NT // 2
    HALF = NT // 2
    LN = 7
    EPS = 1e-5
    HI_BITS = 0xFFFFF000

    x_pairs = x.rearrange("b (q s p) d -> (b q) p s d", s=2, p=P)
    out_pairs = out.rearrange("b (q s p) d -> (b q) p s d", s=2, p=P)
    adj_tiles = adj.rearrange("(t p) n -> t p n", p=P)
    w_rows = W.rearrange("(t p) d -> p t d", p=P)

    ctx = ExitStack()
    with ctx:
        def sb(name, shape, dt):
            return ctx.enter_context(nc.sbuf_tensor(name, shape, dt))

        def pb(name):
            return ctx.enter_context(nc.psum_tensor(name, [P, 512], fp32))

        def sem(name):
            return ctx.enter_context(nc.semaphore(name))

        adjT8 = sb("adjT8", [P, NT, NT, P], i8)
        adjT = [sb(f"adjT{s}", [P, NT, P], fp32r) for s in range(2)]
        mj_hi = sb("mj_hi", [P, NT, DO], fp32r)
        mj_lo = sb("mj_lo", [P, NT, DO], fp32r)
        r = sb("r", [P, NT, DO], fp32)
        WT = sb("WT", [P, 2 * DK, DO], fp32)
        x_in = [sb(f"x_in{s}", [P, 2, D], fp32) for s in range(2)]
        xT = [sb(f"xT{s}", [P, 2, DK, P], fp32) for s in range(2)]
        mj_top = [sb(f"mj_top{s}", [P, DO], fp32) for s in range(2)]
        stage = sb("stage", [P, OT, 2 * D], fp32)
        adj_in = [stage[:, 2 * s:2 * s + 2, :].rearrange("p t d -> p (t d)").bitcast(i32) for s in range(2)]
        adj_bf = [sb(f"adj_bf{s}", [P, N], bf16) for s in range(2)]
        bias = sb("bias", [P, DO], fp32)
        deg = sb("deg", [P, NT], fp32)
        ident = sb("ident", [P, P], fp32)
        ident_bf = sb("ident_bf", [P, P], bf16)
        stats = sb("stats", [P, 6], fp32)
        mean_var = sb("mean_var", [P, 2], fp32)
        var_eps = sb("var_eps", [P, 1], fp32)
        std = sb("std", [P, 1], fp32)
        inv0 = sb("inv0", [P, 1], fp32)
        newton = sb("newton", [P, 2], fp32)
        inv_std = sb("inv_std", [P, 1], fp32)

        aux_ps = [pb(f"aux_ps{s}") for s in range(2)]
        mj_ps = [pb(f"mj_ps{s}") for s in range(2)]
        mi_ps = [pb(f"mi_ps{s}") for s in range(2)]
        agg_ps = [pb(f"agg_ps{s}") for s in range(2)]
        wT_ps = [agg_ps[0], agg_ps[1], aux_ps[0], aux_ps[1]]
        adjT_ps = [a[:, :].bitcast(bf16) for a in aux_ps]

        x_loaded = [sem(f"x_loaded{s}") for s in range(2)]
        w_loaded = [sem("wi_loaded"), sem("wj_loaded")]
        b_loaded = sem("b_loaded")
        adj_loaded = [sem(f"adj_loaded{s}") for s in range(2)]
        out_stored = sem("out_stored")
        zeroed = sem("zeroed")
        ident_ready = sem("ident_ready")
        wT_in_psum = sem("wT_in_psum")
        wT_even = sem("wT_even")
        wT_odd = sem("wT_odd")
        xT_ready = sem("xT_ready")
        mj_ready = sem("mj_ready")
        mi_ready = sem("mi_ready")
        top_ready = sem("top_ready")
        hi_ready = sem("hi_ready")
        lo_ready = sem("lo_ready")
        r_ready = sem("r_ready")
        adj_cast = sem("adj_cast")
        adjT_in_psum = sem("adjT_in_psum")
        adjT8_ready = sem("adjT8_ready")
        adjT_ready = sem("adjT_ready")
        agg_ready = sem("agg_ready")
        degb_ready = sem("degb_ready")
        sum_ready = sem("sum_ready")
        ln_step = sem("ln_step")
        std_ready = sem("std_ready")
        norm_ready = sem("norm_ready")

        block = ctx.enter_context(nc.Block())

        def over_batches(eng, batch):
            batch(0)
            with eng.Fori(1, NB - 1) as bt:
                batch(bt)
            batch(NB - 1)

        def over_groups(eng, bt, group, last_apart=True):
            first = 0
            if isinstance(bt, int) and bt == 0:
                group(0)
                first = 1
            end = NG - 1 if last_apart else NG
            with eng.Fori(first, end) as g:
                group(g)
            if last_apart:
                group(NG - 1)

        def known(*v):
            return all(isinstance(a, int) for a in v)

        @block.sync
        def _(sp):
            def load_pair(q, slot):
                sp.dma_start(x_in[slot][:, :, :], x_pairs[q]).then_inc(x_loaded[slot], 16)

            def load_next(q, slot):
                sp.wait_ge(r_ready, 2 * (q - 1))
                load_pair(q, slot)

            def load_adj(t, slot):
                sp.wait_ge(adj_cast, t - 1)
                sp.dma_start(adj_in[slot], adj_tiles[t]).then_inc(adj_loaded[slot], 16)

            load_pair(0, 0)
            sp.dma_start(stage[:, :, D:], w_rows[:, :, D:]).then_inc(w_loaded[1], 16)
            sp.dma_start(stage[:, :, :D], w_rows[:, :, :D]).then_inc(w_loaded[0], 16)
            sp.dma_start(bias[:, :], b.partition_broadcast(P)).then_inc(b_loaded, 16)
            load_pair(1, 1)
            sp.wait_ge(wT_in_psum, 2 * DK)
            for slot in range(2):
                sp.dma_start(adj_in[slot], adj_tiles[slot]).then_inc(adj_loaded[slot], 16)

            def batch(bt):
                if known(bt) and bt == 0:
                    load_adj(2, 0)
                    load_adj(3, 1)
                    with sp.Fori(1, NG) as g:
                        for s in range(2):
                            load_next(2 * g + s, s)
                            for u in range(2):
                                load_adj(4 * g + 2 * s + u, u)
                else:
                    with sp.Fori(1, NG) as g:
                        for s in range(2):
                            load_next(NP * bt + 2 * g + s, s)
                if not (known(bt) and bt == NB - 1):
                    for s in range(2):
                        load_next(NP * bt + NP + s, s)
                with sp.Fori(0, NP) as k:
                    sp.wait_ge(norm_ready, NT * bt + 2 * k + 2)
                    sp.dma_start(out_pairs[NP * bt + k], r[:, bass.ds(2 * k, 2), :]).then_inc(out_stored, 16)

            over_batches(sp, batch)
            sp.wait_ge(out_stored, 16 * NP * NB)

        @block.gpsimd
        def _(pool):
            for m in (ident, ident_bf):
                pool.memset(m[:, :], 0.0).then_inc(zeroed, 1)
            pool.wait_ge(zeroed, 2)
            for m in (ident, ident_bf):
                pool.affine_select(out=m[:, :], in_=m[:, :], compare_op=ALU.not_equal, fill=1.0, base=0,
                                   pattern=[[-1, P]], channel_multiplier=1).then_inc(ident_ready, 1)

        @block.tensor
        def _(pe):
            def transpose_w(half):
                pe.wait_ge(w_loaded[half], 16)
                for k in range(DK):
                    if half == 0:
                        pe.wait_ge(wT_odd if k % 2 else wT_even, k // 2 + 1)
                    for t in range(OT):
                        last = nc.tensor.transpose(wT_ps[k][:, t * P:(t + 1) * P],
                                                   stage[:, t, half * D + k * P:half * D + (k + 1) * P],
                                                   ident[:, :])
                    last.then_inc(wT_in_psum, 1)

            def transpose_adj(t):
                pe.wait_ge(adj_cast, t + 1)
                for h in range(2):
                    if not (known(t) and t == 0):
                        pe.wait_ge(adjT8_ready, 2 * t - 1 + h)
                    for c in range(HALF):
                        j = h * HALF + c
                        last = nc.tensor.transpose(adjT_ps[h][:, c * P:(c + 1) * P],
                                                   adj_bf[t_slot[0]][:, j * P:(j + 1) * P], ident_bf[:, :])
                    last.then_inc(adjT_in_psum, 1)

            t_slot = [0]

            def project(n, u, dst, half, free, ready, wait_free):
                if wait_free:
                    pe.wait_ge(free, n - 1)
                for k in range(DK):
                    last = nc.tensor.matmul(dst[u % 2][:, :], xT[u // 2][:, u % 2, k, :], WT[:, half * DK + k, :],
                                            start=(k == 0), stop=(k == DK - 1))
                last.then_inc(ready, 1)

            def aggregate(bt, i, s, first, wait_free):
                m = NT * bt + i
                if wait_free:
                    pe.wait_ge(sum_ready, m - 1)
                pe.wait_ge(adjT_ready, m + 1)
                if first:
                    pe.wait_ge(hi_ready, NT * bt + NT - 2)
                for j in range(NT):
                    if first and j >= NT - 2:
                        n = NT * bt + j
                        pe.wait_ge(hi_ready, n + 1)
                        pe.wait_ge(lo_ready, n + 1)
                    for part in (mj_hi, mj_lo):
                        last = nc.tensor.matmul(agg_ps[s][:, :], adjT[s][:, j, :], part[:, j, :],
                                                start=(j == 0 and part is mj_hi),
                                                stop=(j == NT - 1 and part is mj_lo))
                last.then_inc(agg_ready, 1)

            def batch(bt):
                zero = known(bt) and bt == 0

                def group(g):
                    start = zero and known(g) and g == 0
                    for u in range(GT):
                        n = NT * bt + GT * g + u
                        if u % 2 == 0:
                            pe.wait_ge(xT_ready, NP * bt + 2 * g + u // 2 + 1)
                        if start and u == 0:
                            pe.wait_ge(wT_even, DK // 2)
                            pe.wait_ge(wT_odd, DK // 2)
                        project(n, u, mj_ps, 1, lo_ready, mj_ready, not (start and u < 2))
                        if start and u == 0:
                            transpose_w(0)
                            pe.wait_ge(wT_even, DK)
                            pe.wait_ge(wT_odd, DK)
                        project(n, u, mi_ps, 0, r_ready, mi_ready, not (start and u < 2))
                        if zero and not (start and u == 0):
                            t_slot[0] = (u - 1) % 2
                            transpose_adj(GT * g + u - 1)

                over_groups(pe, bt, group, last_apart=False)
                if zero:
                    t_slot[0] = (NT - 1) % 2
                    transpose_adj(NT - 1)

                for i in range(2):
                    aggregate(bt, i, i, i == 0, not (zero))
                with pe.Fori(1, NP) as k:
                    for i in range(2):
                        aggregate(bt, 2 * k + i, i, False, True)

            pe.wait_ge(ident_ready, 2)
            transpose_w(1)
            over_batches(pe, batch)

        @block.scalar
        def _(act):
            def copy_wT(half, k):
                act.wait_ge(wT_in_psum, (1 - half) * DK + k + 1)
                nc.scalar.activation(WT[:, half * DK + k, :], wT_ps[k][:, :], ACT.Copy).then_inc(wT_even, 1)

            def cast_adj(t, s, wait_free):
                if wait_free:
                    act.wait_ge(adjT_in_psum, 2 * t - 2)
                act.wait_ge(adj_loaded[s], 8 * (t - s) + 16)
                nc.scalar.activation(adj_bf[s][:, :], adj_in[s], ACT.Copy,
                                     accum_out=deg[:, bass.ds(t, 1)]).then_inc(adj_cast, 1)

            def copy_adjT(t):
                for h in range(2):
                    act.wait_ge(adjT_in_psum, 2 * t + h + 1)
                    nc.scalar.activation(
                        adjT8[:, bass.ds(t, 1), h * HALF:(h + 1) * HALF, :].rearrange("p a t i -> p (a t i)"),
                        adjT_ps[h], ACT.Copy).then_inc(adjT8_ready, 1)

            def copy_hi(n, t, s):
                act.wait_ge(top_ready, n + 1)
                nc.scalar.activation(mj_hi[:, bass.ds(t, 1), :].rearrange("p t d -> p (t d)"),
                                     mj_top[s][:, :], ACT.Copy).then_inc(hi_ready, 1)

            def widen_adjT(i, s):
                nc.scalar.activation(adjT[s][:, :, :].rearrange("p t i -> p (t i)"),
                                     adjT8[:, bass.ds(i, 1), :, :].rearrange("p a t i -> p (a t i)"),
                                     ACT.Copy).then_inc(adjT_ready, 1)

            def root(m):
                act.wait_ge(ln_step, LN * m + 3)
                nc.scalar.activation(std[:, :], var_eps[:, :], ACT.Sqrt).then_inc(std_ready, 1)

            def batch(bt):
                zero = known(bt) and bt == 0

                def group(g):
                    start = zero and known(g) and g == 0
                    end = known(g) and g == NG - 1
                    if end:
                        for i in range(2):
                            widen_adjT(i, i)
                    for u in range(GT):
                        n = NT * bt + GT * g + u
                        if zero:
                            cast_adj(GT * g + u, u % 2, not (start and u < 2))
                            if not (start and u == 0):
                                copy_adjT(GT * g + u - 1)
                        copy_hi(n, GT * g + u, u % 2)

                over_groups(act, bt, group)
                if zero:
                    copy_adjT(NT - 1)
                with act.Fori(0, NP - 1) as k:
                    for i in range(2):
                        m = NT * bt + 2 * k + i
                        act.wait_ge(agg_ready, m + 1)
                        widen_adjT(2 * k + i + 2, i)
                        root(m)
                for i in range(2):
                    root(NT * bt + NT - 2 + i)

            for half in (1, 0):
                for k in range(0, DK, 2):
                    copy_wT(half, k)
            over_batches(act, batch)

        @block.vector
        def _(dve):
            def copy_wT(half, k):
                dve.wait_ge(wT_in_psum, (1 - half) * DK + k + 1)
                nc.vector.tensor_copy(WT[:, half * DK + k, :], wT_ps[k][:, :]).then_inc(wT_odd, 1)

            def slot(buf, t):
                return buf[:, bass.ds(t, 1), :].rearrange("p t d -> p (t d)")

            def split_mj(n, t, s, wait_free):
                if wait_free:
                    dve.wait_ge(hi_ready, n - 1)
                dve.wait_ge(mj_ready, n + 1)
                nc.vector.tensor_scalar(mj_top[s][:, :].bitcast(u32), mj_ps[s][:, :].bitcast(u32),
                                        HI_BITS, None, ALU.bitwise_and).then_inc(top_ready, 1)
                dve.wait_ge(top_ready, n + 1)
                nc.vector.tensor_tensor(slot(mj_lo, t), mj_ps[s][:, :], mj_top[s][:, :],
                                        ALU.subtract).then_inc(lo_ready, 1)

            def transpose_pair(q, slot, quadrants, slot_value):
                if quadrants[0] == 0:
                    dve.wait_ge(x_loaded[slot], slot_value)
                for a in quadrants:
                    blocks = x_in[slot][a * B:(a + 1) * B, :, :].rearrange("p s (k g c) -> p s k g c", g=Q, c=B)
                    for g in range(Q):
                        last = nc.vector.transpose(xT[slot][g * B:(g + 1) * B, :, :, a * B:(a + 1) * B],
                                                   blocks[:, :, :, g, :])
                if quadrants[-1] == Q - 1:
                    last.then_inc(xT_ready, 1)

            def residual(n, t, u):
                dve.wait_ge(mi_ready, n + 1)
                nc.vector.scalar_tensor_tensor(slot(r, t), mi_ps[u % 2][:, :], deg[:, bass.ds(t, 1)],
                                               x_in[u // 2][:, u % 2, :], ALU.mult, ALU.add).then_inc(r_ready, 1)

            def normalise(m, i, s):
                nc.vector.scalar_tensor_tensor(slot(r, i), bias[:, :], deg[:, bass.ds(i, 1)], slot(r, i),
                                               ALU.mult, ALU.add).then_inc(degb_ready, 1)
                dve.wait_ge(degb_ready, m + 1)
                dve.wait_ge(agg_ready, m + 1)
                nc.vector.tensor_tensor(slot(r, i), agg_ps[s][:, :], slot(r, i), ALU.add).then_inc(sum_ready, 1)
                dve.drain()
                nc.vector.bn_stats(stats[:, :], slot(r, i)).then_inc(ln_step, 1)
                dve.drain()
                nc.vector.bn_aggr(mean_var[:, :], stats[:, :]).then_inc(ln_step, 1)
                dve.wait_ge(ln_step, LN * m + 2)
                nc.vector.tensor_scalar_add(var_eps[:, :], mean_var[:, 1:2], EPS).then_inc(ln_step, 1)
                dve.wait_ge(std_ready, m + 1)
                nc.vector.reciprocal(inv0[:, :], std[:, :]).then_inc(ln_step, 1)
                dve.wait_ge(ln_step, LN * m + 4)
                nc.vector.scalar_tensor_tensor(newton[:, 0:1], inv0[:, :], var_eps[:, :], inv0[:, :],
                                               ALU.mult, ALU.mult).then_inc(ln_step, 1)
                dve.wait_ge(ln_step, LN * m + 5)
                nc.vector.tensor_scalar(newton[:, 1:2], newton[:, 0:1], -0.5, 1.5,
                                        ALU.mult, ALU.add).then_inc(ln_step, 1)
                dve.wait_ge(ln_step, LN * m + 6)
                nc.vector.tensor_tensor(inv_std[:, :], inv0[:, :], newton[:, 1:2], ALU.mult).then_inc(ln_step, 1)
                dve.wait_ge(ln_step, LN * m + 7)
                nc.vector.tensor_scalar(slot(r, i), slot(r, i), mean_var[:, 0:1], inv_std[:, :],
                                        ALU.subtract, ALU.mult).then_inc(norm_ready, 1)

            def batch(bt):
                zero = known(bt) and bt == 0

                def group(g):
                    start = zero and known(g) and g == 0
                    end = known(g) and g == NG - 1
                    for u in range(GT):
                        t = GT * g + u
                        n = NT * bt + t
                        more = u % 2 == 0 and not (end and u == GT - 2)
                        nxt = (NP * bt + 2 * g + u // 2 + 1, (u // 2 + 1) % 2)
                        nxt_value = 16 * (NG * bt + g + 1 + u // 2)
                        split_mj(n, t, u % 2, not (start and u < 2))
                        if more:
                            transpose_pair(*nxt, range(Q // 2), nxt_value)
                        if start and u == 0:
                            for k in range(1, DK, 2):
                                copy_wT(0, k)
                        if zero:
                            dve.wait_ge(adj_cast, t + 1)
                        elif u == 0:
                            dve.wait_ge(out_stored, 16 * NP * bt)
                        residual(n, t, u)
                        if more:
                            transpose_pair(*nxt, range(Q // 2, Q), nxt_value)

                over_groups(dve, bt, group)
                with dve.Fori(0, NP - 1) as k:
                    for i in range(2):
                        normalise(NT * bt + 2 * k + i, 2 * k + i, i)
                if not (known(bt) and bt == NB - 1):
                    transpose_pair(NP * bt + NP, 0, range(Q), 16 * (NG * bt + NG + 1))
                for i in range(2):
                    normalise(NT * bt + NT - 2 + i, NT - 2 + i, i)

            transpose_pair(0, 0, range(Q), 16)
            dve.wait_ge(b_loaded, 16)
            for k in range(1, DK, 2):
                copy_wT(1, k)
            over_batches(dve, batch)


def kernel(**inputs):
    import numpy as _np
    import concourse.bacc as _bacc
    from concourse import mybir as _mybir
    from concourse.bass_utils import run_bass_kernel_spmd as _run

    nc = _bacc.Bacc("TRN2", target_bir_lowering=False, num_devices=1)
    arrays, args = {}, []
    for name in ("x", "adj", "L0_gnn_W", "L0_gnn_b"):
        a = _np.ascontiguousarray(inputs[name])
        arrays[f"in_{name}"] = a
        args.append(nc.dram_tensor(f"in_{name}", a.shape, _mybir.dt.from_np(a.dtype), kind="ExternalInput").ap())
    shape = arrays["in_x"].shape
    args.append(nc.dram_tensor("out_0", shape, _mybir.dt.float32, kind="ExternalOutput").ap())
    bass_adj_resnorm(nc, *args)
    r = _run(nc, [arrays], core_ids=[0])
    return r.results[0]["out_0"]
```

```python
import concourse.bass as bass
from concourse import mybir
from contextlib import ExitStack


def bass_adj_resnorm(nc, x, adj, W, b, out):
    fp32 = mybir.dt.float32
    fp32r = mybir.dt.float32r
    bf16 = mybir.dt.bfloat16
    i32 = mybir.dt.int32
    u32 = mybir.dt.uint32
    u16 = mybir.dt.uint16
    i8 = mybir.dt.int8
    ALU = mybir.AluOpType
    ACT = mybir.ActivationFunctionType

    NB, N, D = x.shape
    DO = W.shape[0]
    P = 128
    NT = N // P
    DK = D // P
    OT = DO // P
    B = 32
    Q = P // B
    GT = 4
    NG = NT // GT
    NP = NT // 2
    WARM_UP = 48
    LN = 7
    EPS = 1e-5
    HI_BITS = 0xFFFFF000

    x_pairs = x.rearrange("b (q p s) d -> (b q) p s d", s=2, p=P)
    out_pairs = out.rearrange("b (q p s) d -> (b q) p s d", s=2, p=P)
    adj_tiles = adj.rearrange("(q p s) n -> q s p n", s=2, p=P)
    w_rows = W.rearrange("(t p) d -> p t d", p=P)

    ctx = ExitStack()
    with ctx:
        def sb(name, shape, dt):
            return ctx.enter_context(nc.sbuf_tensor(name, shape, dt))

        def pb(name):
            return ctx.enter_context(nc.psum_tensor(name, [P, 512], fp32))

        def sem(name):
            return ctx.enter_context(nc.semaphore(name))

        adjT8 = sb("adjT8", [P, NT, NP * P * 2], i8)
        adjT = [sb(f"adjT{s}", [P, NT, P], fp32r) for s in range(2)]
        mj_hi = sb("mj_hi", [P, NT, DO], fp32r)
        mj_lo = sb("mj_lo", [P, NT, DO], fp32r)
        r = sb("r", [P, NT, DO], fp32)
        WT = sb("WT", [P, 2 * DK, DO], fp32)
        x_in = [sb(f"x_in{s}", [P, 2, D], fp32) for s in range(2)]
        xT = [sb(f"xT{s}", [P, 2, DK, P], fp32) for s in range(2)]
        mj_top = [sb(f"mj_top{s}", [P, DO], fp32) for s in range(2)]
        stage = sb("stage", [P, OT, 2 * D], fp32)
        adj_in = [stage[:, 2 * s:2 * s + 2, :].rearrange("p t d -> p (t d)").bitcast(i32) for s in range(2)]
        adj_i8 = [sb(f"adj_i8{s}", [P, N], i8) for s in range(2)]
        bias = sb("bias", [P, DO], fp32)
        deg = sb("deg", [P, NT], fp32)
        ident = sb("ident", [P, P], fp32)
        ident_bf = sb("ident_bf", [P, P], bf16)
        stats = sb("stats", [P, 6], fp32)
        mean_var = sb("mean_var", [P, 2], fp32)
        var_eps = sb("var_eps", [P, 1], fp32)
        std = sb("std", [P, 1], fp32)
        inv0 = sb("inv0", [P, 1], fp32)
        newton = sb("newton", [P, 2], fp32)
        inv_std = sb("inv_std", [P, 1], fp32)

        aux_ps = [pb(f"aux_ps{s}") for s in range(2)]
        mj_ps = [pb(f"mj_ps{s}") for s in range(2)]
        mi_ps = [pb(f"mi_ps{s}") for s in range(2)]
        agg_ps = [pb(f"agg_ps{s}") for s in range(2)]
        wT_ps = [agg_ps[0], agg_ps[1], aux_ps[0], aux_ps[1]]
        adjT_ps = [a[:, :].bitcast(bf16) for a in aux_ps]

        x_loaded = [sem(f"x_loaded{s}") for s in range(2)]
        w_loaded = [sem("wi_loaded"), sem("wj_loaded0"), sem("wj_loaded1")]
        b_loaded = sem("b_loaded")
        x0_loaded = sem("x0_loaded")
        xT0_ready = sem("xT0_ready")
        adj_loaded = [sem(f"adj_loaded{s}") for s in range(2)]
        out_stored = sem("out_stored")
        zeroed = sem("zeroed")
        ident_ready = sem("ident_ready")
        wT_in_psum = sem("wT_in_psum")
        wT_ready = sem("wT_ready")
        xT_ready = sem("xT_ready")
        mj_ready = sem("mj_ready")
        mi_ready = sem("mi_ready")
        top_ready = sem("top_ready")
        hi_ready = sem("hi_ready")
        lo_ready = sem("lo_ready")
        r_ready = sem("r_ready")
        adj_cast = sem("adj_cast")
        adjT_in_psum = sem("adjT_in_psum")
        adjT8_ready = sem("adjT8_ready")
        adjT_ready = sem("adjT_ready")
        agg_ready = sem("agg_ready")
        degb_ready = sem("degb_ready")
        sum_ready = sem("sum_ready")
        ln_step = sem("ln_step")
        std_ready = sem("std_ready")
        norm_ready = sem("norm_ready")

        block = ctx.enter_context(nc.Block())

        def over_batches(eng, batch):
            batch(0)
            with eng.Fori(1, NB - 1) as bt:
                batch(bt)
            batch(NB - 1)

        def over_groups(eng, bt, group, last_apart=True):
            first = 0
            if isinstance(bt, int) and bt == 0:
                group(0)
                first = 1
            end = NG - 1 if last_apart else NG
            with eng.Fori(first, end) as g:
                group(g)
            if last_apart:
                group(NG - 1)

        def known(*v):
            return all(isinstance(a, int) for a in v)

        @block.sync
        def _(sp):
            def load_pair(q, slot):
                sp.dma_start(x_in[slot][:, :, :], x_pairs[q]).then_inc(x_loaded[slot], 16)

            def load_next(q, slot):
                sp.wait_ge(r_ready, 2 * (q - 1))
                load_pair(q, slot)

            def load_adj(q, slot):
                sp.wait_ge(adj_cast, 2 * q + slot - 1)
                sp.dma_start(adj_in[slot], adj_tiles[q, slot]).then_inc(adj_loaded[slot], 16)

            sp.dma_start(x_in[0][:, 0, :], x_pairs[0][:, 0, :]).then_inc(x0_loaded, 16)
            for h in range(2):
                cols = slice(D + h * D // 2, D + (h + 1) * D // 2)
                sp.dma_start(stage[:, :, cols], w_rows[:, :, cols]).then_inc(w_loaded[1 + h], 16)
            sp.dma_start(x_in[0][:, 1, :], x_pairs[0][:, 1, :]).then_inc(x_loaded[0], 16)
            load_pair(1, 1)
            sp.dma_start(stage[:, :, :D], w_rows[:, :, :D]).then_inc(w_loaded[0], 16)
            sp.dma_start(bias[:, :], b.partition_broadcast(P)).then_inc(b_loaded, 16)
            sp.wait_ge(wT_in_psum, 2 * DK)
            for slot in range(2):
                sp.dma_start(adj_in[slot], adj_tiles[0, slot]).then_inc(adj_loaded[slot], 16)

            def batch(bt):
                if known(bt) and bt == 0:
                    load_adj(1, 0)
                    load_adj(1, 1)
                    with sp.Fori(1, NG) as g:
                        for s in range(2):
                            load_next(2 * g + s, s)
                            for u in range(2):
                                load_adj(2 * g + s, u)
                else:
                    with sp.Fori(1, NG) as g:
                        for s in range(2):
                            load_next(NP * bt + 2 * g + s, s)
                if not (known(bt) and bt == NB - 1):
                    for s in range(2):
                        load_next(NP * bt + NP + s, s)
                final = known(bt) and bt == NB - 1
                with sp.Fori(0, NP - 1 if final else NP) as k:
                    sp.wait_ge(norm_ready, NT * bt + 2 * k + 2)
                    sp.dma_start(out_pairs[NP * bt + k], r[:, bass.ds(2 * k, 2), :]).then_inc(out_stored, 16)
                if final:
                    for i in range(NT - 2, NT):
                        sp.wait_ge(norm_ready, NT * bt + i + 1)
                        sp.dma_start(out_pairs[NP * NB - 1][:, i % 2, :], r[:, i, :]).then_inc(out_stored, 16)

            over_batches(sp, batch)
            sp.wait_ge(out_stored, 16 * (NP * NB + 1))

        @block.gpsimd
        def _(pool):
            for m in (ident, ident_bf):
                pool.memset(m[:, :], 0.0).then_inc(zeroed, 1)
            pool.wait_ge(zeroed, 2)
            for m in (ident, ident_bf):
                pool.affine_select(out=m[:, :], in_=m[:, :], compare_op=ALU.not_equal, fill=1.0, base=0,
                                   pattern=[[-1, P]], channel_multiplier=1).then_inc(ident_ready, 1)

        @block.tensor
        def _(pe):
            def transpose_w(half):
                for k in range(DK):
                    if k % (DK // 2) == 0 and (half or not k):
                        pe.wait_ge(w_loaded[half + 2 * k // DK], 16)
                    if half == 0:
                        pe.wait_ge(wT_ready, k + 1)
                    for t in range(OT):
                        last = nc.tensor.transpose(wT_ps[k][:, t * P:(t + 1) * P],
                                                   stage[:, t, half * D + k * P:half * D + (k + 1) * P],
                                                   ident[:, :])
                    last.then_inc(wT_in_psum, 1)

            def transpose_adj(t, slot, wait_free):
                pe.wait_ge(adj_cast, t + 1)
                if wait_free:
                    pe.wait_ge(adjT8_ready, t - 1)
                for q in range(NP):
                    last = nc.tensor.transpose(adjT_ps[slot][:, q * P:(q + 1) * P],
                                               adj_i8[slot][:, :].bitcast(bf16)[:, q * P:(q + 1) * P],
                                               ident_bf[:, :])
                last.then_inc(adjT_in_psum, 1)

            def project(n, u, dst, half, free, ready, wait_free):
                if wait_free:
                    pe.wait_ge(free, n - 1)
                for k in range(DK):
                    last = nc.tensor.matmul(dst[u % 2][:, :], xT[u // 2][:, u % 2, k, :], WT[:, half * DK + k, :],
                                            start=(k == 0), stop=(k == DK - 1))
                last.then_inc(ready, 1)

            def aggregate(bt, i, s, first, wait_free):
                m = NT * bt + i
                if wait_free:
                    pe.wait_ge(sum_ready, m - 1)
                pe.wait_ge(adjT_ready, m + 1)
                if first:
                    pe.wait_ge(hi_ready, NT * bt + NT - 2)
                for j in range(NT):
                    if first and j >= NT - 2:
                        n = NT * bt + j
                        pe.wait_ge(hi_ready, n + 1)
                        pe.wait_ge(lo_ready, n + 1)
                    for part in (mj_hi, mj_lo):
                        last = nc.tensor.matmul(agg_ps[s][:, :], adjT[s][:, j, :], part[:, j, :],
                                                start=(j == 0 and part is mj_hi),
                                                stop=(j == NT - 1 and part is mj_lo))
                last.then_inc(agg_ready, 1)

            def batch(bt):
                zero = known(bt) and bt == 0

                def group(g):
                    start = zero and known(g) and g == 0
                    for u in range(GT):
                        n = NT * bt + GT * g + u
                        if start and u == 0:
                            pe.wait_ge(xT0_ready, 1)
                        elif start and u == 1:
                            pe.wait_ge(xT_ready, 1)
                        elif u % 2 == 0:
                            pe.wait_ge(xT_ready, NP * bt + 2 * g + u // 2 + 1)
                        if start and u == 0:
                            pe.wait_ge(wT_ready, DK)
                        project(n, u, mj_ps, 1, lo_ready, mj_ready, not (start and u < 2))
                        if start and u == 0:
                            transpose_w(0)
                            pe.wait_ge(wT_ready, 2 * DK)
                        project(n, u, mi_ps, 0, r_ready, mi_ready, not (start and u < 2))
                        if zero and not (start and u == 0):
                            transpose_adj(GT * g + u - 1, (u - 1) % 2, not (start and u <= 2))

                over_groups(pe, bt, group, last_apart=False)
                if zero:
                    transpose_adj(NT - 1, (NT - 1) % 2, True)

                for i in range(2):
                    aggregate(bt, i, i, i == 0, not zero)
                with pe.Fori(1, NP) as k:
                    for i in range(2):
                        aggregate(bt, 2 * k + i, i, False, True)

            pe.wait_ge(ident_ready, 2)
            with pe.Fori(0, WARM_UP // 4) as _:
                for _ in range(4):
                    nc.tensor.matmul(mi_ps[0][:, 0:P], ident_bf[:, :], ident_bf[:, :], start=True, stop=True)
            transpose_w(1)
            over_batches(pe, batch)

        @block.scalar
        def _(act):
            def copy_wT(half, k):
                act.wait_ge(wT_in_psum, (1 - half) * DK + k + 1)
                nc.scalar.activation(WT[:, half * DK + k, :], wT_ps[k][:, :], ACT.Copy).then_inc(wT_ready, 1)

            def cast_adj(t, s, wait_free):
                if wait_free:
                    act.wait_ge(adjT_in_psum, t - 1)
                act.wait_ge(adj_loaded[s], 8 * (t - s) + 16)
                nc.scalar.activation(adj_i8[s][:, :], adj_in[s], ACT.Copy,
                                     accum_out=deg[:, bass.ds(t, 1)]).then_inc(adj_cast, 1)

            def copy_adjT(t, slot):
                act.wait_ge(adjT_in_psum, t + 1)
                nc.scalar.activation(adjT8[:, bass.ds(t, 1), :].rearrange("p a n -> p (a n)").bitcast(u16),
                                     adjT_ps[slot].bitcast(u16), ACT.Copy).then_inc(adjT8_ready, 1)

            def copy_hi(n, t, s):
                act.wait_ge(top_ready, n + 1)
                nc.scalar.activation(mj_hi[:, bass.ds(t, 1), :].rearrange("p t d -> p (t d)"),
                                     mj_top[s][:, :], ACT.Copy).then_inc(hi_ready, 1)

            def widen_adjT(i, s):
                nc.scalar.activation(adjT[s][:, :, :].rearrange("p (q s) i -> p q s i", s=2),
                                     adjT8[:, bass.ds(i, 1), :].rearrange("p a (q i s) -> p (a q) s i", s=2, i=P),
                                     ACT.Copy).then_inc(adjT_ready, 1)

            def root(m):
                act.wait_ge(ln_step, LN * m + 3)
                nc.scalar.activation(std[:, :], var_eps[:, :], ACT.Sqrt).then_inc(std_ready, 1)

            def batch(bt):
                zero = known(bt) and bt == 0

                def group(g):
                    start = zero and known(g) and g == 0
                    end = known(g) and g == NG - 1
                    if end:
                        for i in range(2):
                            widen_adjT(i, i)
                    for u in range(GT):
                        n = NT * bt + GT * g + u
                        if zero:
                            cast_adj(GT * g + u, u % 2, not (start and u < 2))
                            if not (start and u == 0):
                                copy_adjT(GT * g + u - 1, (u - 1) % 2)
                        copy_hi(n, GT * g + u, u % 2)

                over_groups(act, bt, group)
                if zero:
                    copy_adjT(NT - 1, (NT - 1) % 2)
                with act.Fori(0, NP - 1) as k:
                    for i in range(2):
                        m = NT * bt + 2 * k + i
                        act.wait_ge(agg_ready, m + 1)
                        widen_adjT(2 * k + i + 2, i)
                        root(m)
                for i in range(2):
                    root(NT * bt + NT - 2 + i)

            for half in (1, 0):
                for k in range(DK):
                    copy_wT(half, k)
            over_batches(act, batch)

        @block.vector
        def _(dve):
            def slot(buf, t):
                return buf[:, bass.ds(t, 1), :].rearrange("p t d -> p (t d)")

            def split_mj(n, t, s, wait_free):
                if wait_free:
                    dve.wait_ge(hi_ready, n - 1)
                dve.wait_ge(mj_ready, n + 1)
                nc.vector.tensor_scalar(mj_top[s][:, :].bitcast(u32), mj_ps[s][:, :].bitcast(u32),
                                        HI_BITS, None, ALU.bitwise_and).then_inc(top_ready, 1)
                dve.wait_ge(top_ready, n + 1)
                nc.vector.tensor_tensor(slot(mj_lo, t), mj_ps[s][:, :], mj_top[s][:, :],
                                        ALU.subtract).then_inc(lo_ready, 1)

            def transpose_pair(q, slot, quadrants, slot_value):
                if quadrants[0] == 0:
                    dve.wait_ge(x_loaded[slot], slot_value)
                for a in quadrants:
                    blocks = x_in[slot][a * B:(a + 1) * B, :, :].rearrange("p s (k g c) -> p s k g c", g=Q, c=B)
                    for g in range(Q):
                        last = nc.vector.transpose(xT[slot][g * B:(g + 1) * B, :, :, a * B:(a + 1) * B],
                                                   blocks[:, :, :, g, :])
                if quadrants[-1] == Q - 1:
                    last.then_inc(xT_ready, 1)

            def residual(n, t, u):
                dve.wait_ge(mi_ready, n + 1)
                nc.vector.scalar_tensor_tensor(slot(r, t), mi_ps[u % 2][:, :], deg[:, bass.ds(t, 1)],
                                               x_in[u // 2][:, u % 2, :], ALU.mult, ALU.add).then_inc(r_ready, 1)

            def normalise(m, i, s):
                nc.vector.scalar_tensor_tensor(slot(r, i), bias[:, :], deg[:, bass.ds(i, 1)], slot(r, i),
                                               ALU.mult, ALU.add).then_inc(degb_ready, 1)
                dve.wait_ge(degb_ready, m + 1)
                dve.wait_ge(agg_ready, m + 1)
                nc.vector.tensor_tensor(slot(r, i), agg_ps[s][:, :], slot(r, i), ALU.add).then_inc(sum_ready, 1)
                dve.drain()
                nc.vector.bn_stats(stats[:, :], slot(r, i)).then_inc(ln_step, 1)
                dve.drain()
                nc.vector.bn_aggr(mean_var[:, :], stats[:, :]).then_inc(ln_step, 1)
                dve.wait_ge(ln_step, LN * m + 2)
                nc.vector.tensor_scalar_add(var_eps[:, :], mean_var[:, 1:2], EPS).then_inc(ln_step, 1)
                dve.wait_ge(std_ready, m + 1)
                nc.vector.reciprocal(inv0[:, :], std[:, :]).then_inc(ln_step, 1)
                dve.wait_ge(ln_step, LN * m + 4)
                nc.vector.scalar_tensor_tensor(newton[:, 0:1], inv0[:, :], var_eps[:, :], inv0[:, :],
                                               ALU.mult, ALU.mult).then_inc(ln_step, 1)
                dve.wait_ge(ln_step, LN * m + 5)
                nc.vector.tensor_scalar(newton[:, 1:2], newton[:, 0:1], -0.5, 1.5,
                                        ALU.mult, ALU.add).then_inc(ln_step, 1)
                dve.wait_ge(ln_step, LN * m + 6)
                nc.vector.tensor_tensor(inv_std[:, :], inv0[:, :], newton[:, 1:2], ALU.mult).then_inc(ln_step, 1)
                dve.wait_ge(ln_step, LN * m + 7)
                nc.vector.tensor_scalar(slot(r, i), slot(r, i), mean_var[:, 0:1], inv_std[:, :],
                                        ALU.subtract, ALU.mult).then_inc(norm_ready, 1)

            def batch(bt):
                zero = known(bt) and bt == 0

                def group(g):
                    start = zero and known(g) and g == 0
                    end = known(g) and g == NG - 1
                    for u in range(GT):
                        t = GT * g + u
                        n = NT * bt + t
                        more = u % 2 == 0 and not (end and u == GT - 2)
                        nxt = (NP * bt + 2 * g + u // 2 + 1, (u // 2 + 1) % 2)
                        nxt_value = 16 * (NG * bt + g + 1 + u // 2)
                        split_mj(n, t, u % 2, not (start and u < 2))
                        if more:
                            transpose_pair(*nxt, range(Q // 2), nxt_value)
                        if start and u == 0:
                            transpose_pair(*nxt, range(Q // 2, Q), nxt_value)
                        if zero:
                            dve.wait_ge(adj_cast, t + 1)
                        elif u == 0:
                            dve.wait_ge(out_stored, 16 * NP * bt)
                        residual(n, t, u)
                        if more and not (start and u == 0):
                            transpose_pair(*nxt, range(Q // 2, Q), nxt_value)

                over_groups(dve, bt, group)
                if zero:
                    dve.wait_ge(b_loaded, 16)
                with dve.Fori(0, NP - 1) as k:
                    for i in range(2):
                        normalise(NT * bt + 2 * k + i, 2 * k + i, i)
                if not (known(bt) and bt == NB - 1):
                    transpose_pair(NP * bt + NP, 0, range(Q), 16 * (NG * bt + NG + 1))
                for i in range(2):
                    normalise(NT * bt + NT - 2 + i, NT - 2 + i, i)

            for tile, loaded, ready in ((0, x0_loaded, xT0_ready), (1, x_loaded[0], xT_ready)):
                dve.wait_ge(loaded, 16)
                for a in range(Q):
                    blocks = x_in[0][a * B:(a + 1) * B, tile, :].rearrange("p (k g c) -> p k g c", g=Q, c=B)
                    for g in range(Q):
                        last = nc.vector.transpose(xT[0][g * B:(g + 1) * B, tile, :, a * B:(a + 1) * B],
                                                   blocks[:, :, g, :])
                last.then_inc(ready, 1)
            over_batches(dve, batch)


def kernel(**inputs):
    import numpy as _np
    import concourse.bacc as _bacc
    from concourse import mybir as _mybir
    from concourse.bass_utils import run_bass_kernel_spmd as _run

    nc = _bacc.Bacc("TRN2", target_bir_lowering=False, num_devices=1)
    arrays, args = {}, []
    for name in ("x", "adj", "L0_gnn_W", "L0_gnn_b"):
        a = _np.ascontiguousarray(inputs[name])
        arrays[f"in_{name}"] = a
        args.append(nc.dram_tensor(f"in_{name}", a.shape, _mybir.dt.from_np(a.dtype), kind="ExternalInput").ap())
    shape = arrays["in_x"].shape
    args.append(nc.dram_tensor("out_0", shape, _mybir.dt.float32, kind="ExternalOutput").ap())
    bass_adj_resnorm(nc, *args)
    r = _run(nc, [arrays], core_ids=[0])
    return r.results[0]["out_0"]
```
